# Optimizing a Trainium2 kernel written in Bass

```python
import numpy as np
import jax
import jax.numpy as jnp

def _softmax(x, axis=-1):
    return jax.nn.softmax(x, axis=axis)

def _gelu(x):
    return jax.nn.gelu(x, approximate=True)

def _silu(x):
    return jax.nn.silu(x)

def _sigmoid(x):
    return jax.nn.sigmoid(x)

def _layernorm(x, axis=-1, eps=1e-05):
    m = jnp.mean(x, axis=axis, keepdims=True)
    v = jnp.var(x, axis=axis, keepdims=True)
    return (x - m) / jnp.sqrt(v + eps)

def _scatter_add(tgt, idx, src, axis=0):
    return tgt.at[idx].add(src)

def _segment_sum(src, seg, n):
    return jax.ops.segment_sum(src, seg, n)
kernel_name = 'mk_dlrm_tower_d1_rec_r8_143b3e'

def setup_inputs(seed: int=0):
    np.random.seed(seed)
    _w = jnp.asarray

    def _rec_inputs():
        import jax
        import jax.numpy as jnp
        _tk = jax.random.key(seed)
        ids = jnp.stack([jax.random.randint(jax.random.fold_in(_tk, 200 + f), (512,), 0, v, jnp.int32) for f, v in enumerate([125000, 1250, 1000, 12500, 1250, 12500, 1000, 12500, 1250, 12500, 1250, 12500, 1250, 1250, 1000, 1000, 1000, 12500, 1000, 1250, 12500, 1250, 12500, 1000, 1250, 1000])], axis=1)
        tbl_0 = 0.05 * jax.random.normal(jax.random.fold_in(_tk, 500 + 0), (125000, 128), jnp.float32)
        tbl_1 = 0.05 * jax.random.normal(jax.random.fold_in(_tk, 500 + 1), (1250, 128), jnp.float32)
        tbl_2 = 0.05 * jax.random.normal(jax.random.fold_in(_tk, 500 + 2), (1000, 128), jnp.float32)
        tbl_3 = 0.05 * jax.random.normal(jax.random.fold_in(_tk, 500 + 3), (12500, 128), jnp.float32)
        tbl_4 = 0.05 * jax.random.normal(jax.random.fold_in(_tk, 500 + 4), (1250, 128), jnp.float32)
        tbl_5 = 0.05 * jax.random.normal(jax.random.fold_in(_tk, 500 + 5), (12500, 128), jnp.float32)
        tbl_6 = 0.05 * jax.random.normal(jax.random.fold_in(_tk, 500 + 6), (1000, 128), jnp.float32)
        tbl_7 = 0.05 * jax.random.normal(jax.random.fold_in(_tk, 500 + 7), (12500, 128), jnp.float32)
        tbl_8 = 0.05 * jax.random.normal(jax.random.fold_in(_tk, 500 + 8), (1250, 128), jnp.float32)
        tbl_9 = 0.05 * jax.random.normal(jax.random.fold_in(_tk, 500 + 9), (12500, 128), jnp.float32)
        tbl_10 = 0.05 * jax.random.normal(jax.random.fold_in(_tk, 500 + 10), (1250, 128), jnp.float32)
        tbl_11 = 0.05 * jax.random.normal(jax.random.fold_in(_tk, 500 + 11), (12500, 128), jnp.float32)
        tbl_12 = 0.05 * jax.random.normal(jax.random.fold_in(_tk, 500 + 12), (1250, 128), jnp.float32)
        tbl_13 = 0.05 * jax.random.normal(jax.random.fold_in(_tk, 500 + 13), (1250, 128), jnp.float32)
        tbl_14 = 0.05 * jax.random.normal(jax.random.fold_in(_tk, 500 + 14), (1000, 128), jnp.float32)
        tbl_15 = 0.05 * jax.random.normal(jax.random.fold_in(_tk, 500 + 15), (1000, 128), jnp.float32)
        tbl_16 = 0.05 * jax.random.normal(jax.random.fold_in(_tk, 500 + 16), (1000, 128), jnp.float32)
        tbl_17 = 0.05 * jax.random.normal(jax.random.fold_in(_tk, 500 + 17), (12500, 128), jnp.float32)
        tbl_18 = 0.05 * jax.random.normal(jax.random.fold_in(_tk, 500 + 18), (1000, 128), jnp.float32)
        tbl_19 = 0.05 * jax.random.normal(jax.random.fold_in(_tk, 500 + 19), (1250, 128), jnp.float32)
        tbl_20 = 0.05 * jax.random.normal(jax.random.fold_in(_tk, 500 + 20), (12500, 128), jnp.float32)
        tbl_21 = 0.05 * jax.random.normal(jax.random.fold_in(_tk, 500 + 21), (1250, 128), jnp.float32)
        tbl_22 = 0.05 * jax.random.normal(jax.random.fold_in(_tk, 500 + 22), (12500, 128), jnp.float32)
        tbl_23 = 0.05 * jax.random.normal(jax.random.fold_in(_tk, 500 + 23), (1000, 128), jnp.float32)
        tbl_24 = 0.05 * jax.random.normal(jax.random.fold_in(_tk, 500 + 24), (1250, 128), jnp.float32)
        tbl_25 = 0.05 * jax.random.normal(jax.random.fold_in(_tk, 500 + 25), (1000, 128), jnp.float32)
        _rk = jax.random.fold_in(_tk, 7)
        r_bottom_output = -0.000520686 + 1.00062 * jax.random.normal(jax.random.fold_in(_rk, 101), (512, 128), jnp.float32)
        W_top1 = 0.0456912 * jax.random.normal(jax.random.fold_in(_tk, 801), (479, 512), jnp.float32)
        W_top2 = 0.0441942 * jax.random.normal(jax.random.fold_in(_tk, 802), (512, 256), jnp.float32)
        W_top3 = 0.0625 * jax.random.normal(jax.random.fold_in(_tk, 803), (256, 1), jnp.float32)
        b_top1 = jnp.zeros((512,), jnp.float32)
        b_top2 = jnp.zeros((256,), jnp.float32)
        return (r_bottom_output, ids, tbl_0, tbl_1, tbl_2, tbl_3, tbl_4, tbl_5, tbl_6, tbl_7, tbl_8, tbl_9, tbl_10, tbl_11, tbl_12, tbl_13, tbl_14, tbl_15, tbl_16, tbl_17, tbl_18, tbl_19, tbl_20, tbl_21, tbl_22, tbl_23, tbl_24, tbl_25, W_top1, b_top1, W_top2, b_top2, W_top3)
    r_bottom_output, ids, tbl_0, tbl_1, tbl_2, tbl_3, tbl_4, tbl_5, tbl_6, tbl_7, tbl_8, tbl_9, tbl_10, tbl_11, tbl_12, tbl_13, tbl_14, tbl_15, tbl_16, tbl_17, tbl_18, tbl_19, tbl_20, tbl_21, tbl_22, tbl_23, tbl_24, tbl_25, W_top1, b_top1, W_top2, b_top2, W_top3 = _rec_inputs()

    def _L0_rec_setup():
        import jax, jax.numpy as jnp
        import numpy as np
        NUM_FEATURES = 27
        _TRIU_I, _TRIU_J = np.triu_indices(NUM_FEATURES, k=1)
        key = jax.random.key(seed)
        k1, k2 = jax.random.split(key)
        bottom_output = jax.random.normal(k1, (2048, 128), dtype=jnp.float32)
        embeddings = jax.random.normal(k2, (2048, 26, 128), dtype=jnp.float32)
        return {'bottom_output': bottom_output, 'embeddings': embeddings}
    _L0_rec_all = _L0_rec_setup()
    _L0_rec_in = {k: v for k, v in _L0_rec_all.items() if k in ()}
    del _L0_rec_all
    return {'r_bottom_output': r_bottom_output, 'ids': ids, 'tbl_0': tbl_0, 'tbl_1': tbl_1, 'tbl_2': tbl_2, 'tbl_3': tbl_3, 'tbl_4': tbl_4, 'tbl_5': tbl_5, 'tbl_6': tbl_6, 'tbl_7': tbl_7, 'tbl_8': tbl_8, 'tbl_9': tbl_9, 'tbl_10': tbl_10, 'tbl_11': tbl_11, 'tbl_12': tbl_12, 'tbl_13': tbl_13, 'tbl_14': tbl_14, 'tbl_15': tbl_15, 'tbl_16': tbl_16, 'tbl_17': tbl_17, 'tbl_18': tbl_18, 'tbl_19': tbl_19, 'tbl_20': tbl_20, 'tbl_21': tbl_21, 'tbl_22': tbl_22, 'tbl_23': tbl_23, 'tbl_24': tbl_24, 'tbl_25': tbl_25, 'W_top1': W_top1, 'b_top1': b_top1, 'W_top2': W_top2, 'b_top2': b_top2, 'W_top3': W_top3}

def reference(r_bottom_output, ids, tbl_0, tbl_1, tbl_2, tbl_3, tbl_4, tbl_5, tbl_6, tbl_7, tbl_8, tbl_9, tbl_10, tbl_11, tbl_12, tbl_13, tbl_14, tbl_15, tbl_16, tbl_17, tbl_18, tbl_19, tbl_20, tbl_21, tbl_22, tbl_23, tbl_24, tbl_25, W_top1, b_top1, W_top2, b_top2, W_top3):
    import jax
    import jax.numpy as jnp

    def _L0_rec_ref(bottom_output, embeddings):
        import jax, jax.numpy as jnp
        import numpy as np
        NUM_FEATURES = 27
        _TRIU_I, _TRIU_J = np.triu_indices(NUM_FEATURES, k=1)
        all_emb = jnp.concatenate([bottom_output[:, None, :], embeddings], axis=1)
        gram = jnp.einsum('bfd,bgd->bfg', all_emb, all_emb)
        return gram[:, _TRIU_I, _TRIU_J]
    e = jnp.stack([tbl_0[ids[:, 0]], tbl_1[ids[:, 1]], tbl_2[ids[:, 2]], tbl_3[ids[:, 3]], tbl_4[ids[:, 4]], tbl_5[ids[:, 5]], tbl_6[ids[:, 6]], tbl_7[ids[:, 7]], tbl_8[ids[:, 8]], tbl_9[ids[:, 9]], tbl_10[ids[:, 10]], tbl_11[ids[:, 11]], tbl_12[ids[:, 12]], tbl_13[ids[:, 13]], tbl_14[ids[:, 14]], tbl_15[ids[:, 15]], tbl_16[ids[:, 16]], tbl_17[ids[:, 17]], tbl_18[ids[:, 18]], tbl_19[ids[:, 19]], tbl_20[ids[:, 20]], tbl_21[ids[:, 21]], tbl_22[ids[:, 22]], tbl_23[ids[:, 23]], tbl_24[ids[:, 24]], tbl_25[ids[:, 25]]], axis=1)
    z = _L0_rec_ref(r_bottom_output, e)
    z = z.reshape(z.shape[0], -1)
    h = jnp.concatenate([z, r_bottom_output], axis=1)
    h = jnp.maximum(h @ W_top1 + b_top1, 0.0)
    h = jnp.maximum(h @ W_top2 + b_top2, 0.0)
    y = h @ W_top3
    return y

_drawn_inputs = setup_inputs


def setup_inputs(seed=0):
    import zlib

    import numpy as np

    out = dict(_drawn_inputs(seed))
    spreads = {'b_top1': (0.0, 0.1), 'b_top2': (0.0, 0.1)}
    factors = {}
    for name, (base, spread) in spreads.items():
        noise = np.random.default_rng([zlib.crc32(name.encode()), seed]).standard_normal(out[name].shape)
        drawn = base * np.exp(spread * noise) if base else spread * noise
        out[name] = jnp.asarray(drawn.astype(out[name].dtype))
    for name, factor in factors.items():
        out[name] = (out[name] * factor).astype(out[name].dtype)
    return out
```

```python
from contextlib import ExitStack

import concourse.bass as bass
from concourse import mybir

F32 = mybir.dt.float32
F32R = mybir.dt.float32r
I32 = mybir.dt.int32
ACT = mybir.ActivationFunctionType
ALU = mybir.AluOpType

P = 128
D = 128
B = 512
TILES = B // P
F = 27
H1, H2 = 512, 256
TABLE_ROWS = [125000, 1250, 1000, 12500, 1250, 12500, 1000, 12500, 1250, 12500, 1250, 12500, 1250,
              1250, 1000, 1000, 1000, 12500, 1000, 1250, 12500, 1250, 12500, 1000, 1250, 1000]

ONE_HOT_PAIRS = [(2, 6), (14, 15), (16, 18), (23, 25), (21, 24)]
OH_P = 125
ONE_HOT = [f for pair in ONE_HOT_PAIRS for f in pair]
CHUNKS = [TABLE_ROWS[a] // OH_P for a, _ in ONE_HOT_PAIRS]
PAIRS = len(ONE_HOT_PAIRS)
MAX_CHUNKS = max(CHUNKS)
GATHERED = [f for f in range(F - 1) if f not in ONE_HOT]
QUAD = 4
QUADS_PER_TILE = len(GATHERED) // QUAD
QUADS = TILES * QUADS_PER_TILE
SLOT_FEATURE = [f + 1 for f in GATHERED] + [f + 1 for f in ONE_HOT] + [0]
BOTTOM_SLOT = F - 1

J, I = 4, 32
HALF = I // 2
GRAM_M = 32
ET_ROW = P * F + GRAM_M - F

K_STEPS = 14
F_PER_CHUNK = 9
Z_CHUNKS = 3
Z_FS = [9, 9, 8]
Z_ROWS = [n * K_STEPS for n in Z_FS]

OH_RING = 4


def program(nc, ids_rows, ids_cols, tables, bottom_t, w1_pairs, w1_bottom, b1, w2, b2, w3, out):
    dump = nc.dram_tensor("gram_dump", (TILES, F, F, P), F32, kind="Internal").ap()

    ctx = ExitStack()
    with ctx:
        def sb(name, shape, dt=F32):
            return ctx.enter_context(nc.sbuf_tensor(name, shape, dt))

        def sem(name):
            return ctx.enter_context(nc.semaphore(name))

        ids_sb = sb("ids_sb", [P, TILES * len(GATHERED)], I32)
        rows_sb = sb("rows_sb", [P, 2, len(GATHERED), D])
        ident = sb("ident", [P, P])
        feat = sb("feat", [P, TILES, ET_ROW])
        raw = sb("raw", [OH_P, 2, 2 * MAX_CHUNKS * D])
        hi = sb("hi", [OH_P, 2, 2 * MAX_CHUNKS * D], F32R)
        lo = sb("lo", [OH_P, 2, 2 * MAX_CHUNKS * D], F32R)
        ids_bc = sb("ids_bc", [OH_P, PAIRS, 2 * B], I32)
        row_no = {m: sb(f"row_no_{m}", [OH_P, m]) for m in sorted(set(CHUNKS))}
        one_hot = sb("one_hot", [OH_P, OH_RING, 2 * B], F32R)
        bottom_sb = sb("bottom_sb", [P, B])
        gram_sb = sb("gram_sb", [P, 2, F, I])
        z = sb("z", [P, 2, Z_CHUNKS, P])
        w1p_sb = sb("w1p_sb", [P, Z_CHUNKS, H1])
        w1b_sb = sb("w1b_sb", [P, H1])
        w2_sb = sb("w2_sb", [P, H1 // P, H2])
        w3_sb = sb("w3_sb", [P, H2 // P])
        b1_sb = sb("b1_sb", [P, H1 // P])
        b2_sb = sb("b2_sb", [P, H2 // P])
        h1_sb = sb("h1_sb", [P, 2, H1 // P, P])
        h2_sb = sb("h2_sb", [P, 2, H2 // P, P])
        y_sb = sb("y_sb", [1, B])

        bank = [ctx.enter_context(nc.psum_tensor(f"bank{i}", [P, 512], F32)) for i in range(8)]
        oh_bank = [[bank[0], bank[1]], [bank[2], bank[3]]]
        tr_bank = [bank[4], bank[5]]
        gram_bank = [bank[6], bank[7]]
        h1_bank = [bank[2], bank[3]]
        h2_bank = [bank[0], bank[1]]
        y_ps = bank[0][0:1, P:2 * P]

        s_ids = sem("s_ids")
        s_rows = [sem(f"s_rows{q}") for q in range(QUADS)]
        s_raw = [sem(f"s_raw{i}") for i in range(2)]
        s_ids_bc = [sem(f"s_ids_bc{g}") for g in range(PAIRS)]
        s_weights = sem("s_weights")
        s_bottom = sem("s_bottom")
        s_row_no = sem("s_row_no")
        s_ident = sem("s_ident")
        s_pad = sem("s_pad")
        s_hi = sem("s_hi")
        s_lo = sem("s_lo")
        s_one_hot = sem("s_one_hot")
        s_one_hot_used = sem("s_one_hot_used")
        s_lookup = sem("s_lookup")
        s_bottom_in = sem("s_bottom_in")
        s_transposed = sem("s_transposed")
        s_quad_in = sem("s_quad_in")
        s_gram = sem("s_gram")
        s_gram_a = sem("s_gram_a")
        s_gram_b = sem("s_gram_b")
        s_dump = [sem(f"s_dump{t}") for t in range(TILES)]
        s_z = [sem(f"s_z{t}") for t in range(TILES)]
        s_l1 = sem("s_l1")
        s_h1_act = sem("s_h1_act")
        s_h1_dve = sem("s_h1_dve")
        s_l2 = sem("s_l2")
        s_h2_act = sem("s_h2_act")
        s_h2_dve = sem("s_h2_dve")
        s_l3 = sem("s_l3")
        s_y = sem("s_y")
        s_out = sem("s_out")

        block = ctx.enter_context(nc.Block())
        chunk_base = [sum(CHUNKS[:g]) for g in range(PAIRS + 1)]
        all_chunks = chunk_base[PAIRS]
        N_L1, N_L2 = H1 // P, H2 // P

        def unit_ps(banks, n_units, n):
            half, nth = divmod(n, n_units // 2)
            return banks[half][:, nth * P:(nth + 1) * P]

        def dump_and_regroup(eng, t):
            eng.wait_ge(s_gram_a, t + 1)
            eng.wait_ge(s_gram_b, t + 1)
            for j in range(J):
                eng.dma_start(dump[t, :, :, j * I:(j + 1) * I],
                              gram_sb[j * GRAM_M:j * GRAM_M + F, t % 2, :, :]).then_inc(s_dump[t], 16)
            eng.wait_ge(s_dump[t], 16 * J)
            if t >= 2:
                eng.wait_ge(s_l1, 2 * (t - 1))
            for c in range(Z_CHUNKS):
                src = bass.AP(dump.tensor, t * F * F * P + c * F_PER_CHUNK * (F + 1) * P + P,
                              [[(F + 1) * P, Z_FS[c]], [P, K_STEPS], [1, P]])
                eng.dma_start(z[0:Z_ROWS[c], t % 2, c, :], src).then_inc(s_z[t], 16)

        @block.sync
        def _(sp):
            sp.dma_start(ids_sb[:, :], ids_rows).then_inc(s_ids, 16)
            for g in range(PAIRS):
                if g >= 2:
                    sp.wait_ge(s_lo, g - 1)
                n = CHUNKS[g] * D
                for e in range(2):
                    src = tables[ONE_HOT_PAIRS[g][e]].rearrange("(p c) d -> p (c d)", p=OH_P)
                    sp.dma_start(raw[:, g % 2, e * n:(e + 1) * n], src).then_inc(s_raw[g % 2], 16)
            for t in range(TILES):
                dump_and_regroup(sp, t)
            sp.wait_ge(s_y, TILES)
            sp.dma_start(out.rearrange("(a b) n -> a (b n)", a=1), y_sb[:, :]).then_inc(s_out, 16)
            sp.wait_ge(s_out, 16)

        @block.gpsimd
        def _(pool):
            pool.memset(ident[:, :], 0.0).then_inc(s_ident, 1)
            for m in row_no:
                pool.iota(row_no[m][:, :], pattern=[[1, m]], base=0, channel_multiplier=m,
                          allow_small_or_imprecise_dtypes=True).then_inc(s_row_no, 1)
            pool.wait_ge(s_ident, 1)
            pool.affine_select(out=ident[:, :], in_=ident[:, :], compare_op=ALU.not_equal, fill=1.0,
                               base=0, pattern=[[-1, P]], channel_multiplier=1).then_inc(s_ident, 1)
            pool.wait_ge(s_ids, 16)
            for q in range(QUADS):
                t = q // QUADS_PER_TILE
                if t >= 2:
                    pool.wait_ge(s_transposed, q - 2 * QUADS_PER_TILE + 1)
                for n in range(QUAD):
                    s = q % QUADS_PER_TILE * QUAD + n
                    at = t * len(GATHERED) + s
                    pool.indirect_dma_start(
                        out=rows_sb[:, t % 2, s, :], out_offset=None, in_=tables[GATHERED[s]][:, :],
                        in_offset=bass.IndirectOffsetOnAxis(ap=ids_sb[:, at:at + 1], axis=0),
                    ).then_inc(s_rows[q], 16)

        @block.tensor
        def _(pe):
            def lookup(g):
                pe.wait_ge(s_lo, g + 1)
                if g >= 2:
                    pe.wait_ge(s_lookup, 2 * (g - 1))
                m = CHUNKS[g]
                for c in range(m):
                    pe.wait_ge(s_one_hot, chunk_base[g] + c + 1)
                    for e in range(2):
                        col = (e * m + c) * D
                        for part in (hi, lo):
                            last = pe.matmul(oh_bank[g % 2][e][:, :], lhsT=part[:, g % 2, col:col + D],
                                             rhs=one_hot[:, (chunk_base[g] + c) % OH_RING, e * B:(e + 1) * B],
                                             start=(c == 0 and part is hi), stop=(c == m - 1 and part is lo))
                    last.then_inc(s_one_hot_used, 1)

            def transpose(q):
                pe.wait_ge(s_rows[q], 16 * QUAD)
                if q >= 2:
                    pe.wait_ge(s_quad_in, q - 1)
                t = q // QUADS_PER_TILE
                for n in range(QUAD):
                    s = q % QUADS_PER_TILE * QUAD + n
                    last = pe.transpose(tr_bank[q % 2][:, n * P:(n + 1) * P], rows_sb[:, t % 2, s, :], ident[:, :])
                last.then_inc(s_transposed, 1)

            def gram(t):
                pe.wait_ge(s_quad_in, QUADS_PER_TILE * (t + 1))
                pe.wait_ge(s_lookup, 2 * PAIRS)
                pe.wait_ge(s_bottom_in, 1)
                pe.wait_ge(s_pad, 1)
                for half in range(2):
                    if t >= 1:
                        pe.wait_ge(s_gram_a if half == 0 else s_gram_b, t)
                    for i in range(HALF):
                        for j in range(J):
                            at = (j * I + half * HALF + i) * F
                            last = pe.matmul(
                                gram_bank[half][j * GRAM_M:(j + 1) * GRAM_M, i * F:(i + 1) * F],
                                lhsT=feat[:, t, at:at + GRAM_M], rhs=feat[:, t, at:at + F],
                                start=True, stop=True, tile_position=(0, j * GRAM_M))
                    last.then_inc(s_gram, 1)

            def mlp(t):
                if t == 0:
                    pe.wait_ge(s_weights, 16 * 6)
                    pe.wait_ge(s_bottom, 16)
                else:
                    pe.wait_ge(s_h1_act, N_L1 // 2 * t)
                    pe.wait_ge(s_h1_dve, N_L1 // 2 * t)
                for n in range(N_L1):
                    pe.matmul(unit_ps(h1_bank, N_L1, n), lhsT=w1b_sb[:, n * P:(n + 1) * P],
                              rhs=bottom_sb[:, t * P:(t + 1) * P], start=(n % (N_L1 // 2) == 0), stop=False,
                              skip_group_check=True)
                pe.wait_ge(s_z[t], 16 * Z_CHUNKS)
                for n in range(N_L1):
                    for c in range(Z_CHUNKS):
                        k = Z_ROWS[c]
                        last = pe.matmul(unit_ps(h1_bank, N_L1, n), lhsT=w1p_sb[0:k, c, n * P:(n + 1) * P],
                                         rhs=z[0:k, t % 2, c, :], start=False, stop=(c == Z_CHUNKS - 1),
                                         skip_group_check=True)
                    if n % (N_L1 // 2) == N_L1 // 2 - 1:
                        last.then_inc(s_l1, 1)
                if t >= 1:
                    pe.wait_ge(s_y, t)
                for k in range(N_L1):
                    half, nth = divmod(k, N_L1 // 2)
                    pe.wait_ge(s_h1_dve if half else s_h1_act, N_L1 // 2 * t + nth + 1)
                    for n in range(N_L2):
                        last = pe.matmul(unit_ps(h2_bank, N_L2, n), lhsT=w2_sb[:, k, n * P:(n + 1) * P],
                                         rhs=h1_sb[:, t % 2, k, :], start=(k == 0),
                                         stop=(k == N_L1 - 1), skip_group_check=True)
                last.then_inc(s_l2, 1)
                pe.wait_ge(s_h2_act, t + 1)
                pe.matmul(y_ps, lhsT=w3_sb[:, 0:1], rhs=h2_sb[:, t % 2, 0, :], start=True, stop=False)
                pe.wait_ge(s_h2_dve, t + 1)
                pe.matmul(y_ps, lhsT=w3_sb[:, 1:2], rhs=h2_sb[:, t % 2, 1, :], start=False,
                          stop=True).then_inc(s_l3, 1)

            pe.wait_ge(s_ident, 2)
            for step, n in PLAN:
                {"lookup": lookup, "quad": transpose, "gram": gram, "mlp": mlp}[step](n)

        @block.scalar
        def _(act):
            def split_hi(g):
                act.wait_ge(s_raw[g % 2], 32 * (g // 2 + 1))
                if g >= 2:
                    act.wait_ge(s_one_hot_used, chunk_base[g - 1])
                n = 2 * CHUNKS[g] * D
                act.activation(hi[:, g % 2, 0:n], raw[:, g % 2, 0:n], ACT.Copy).then_inc(s_hi, 1)

            def lookup_out(g):
                act.wait_ge(s_one_hot_used, chunk_base[g + 1])
                for e in range(2):
                    slot = len(GATHERED) + 2 * g + e
                    dst = feat[:, :, slot:slot + (P - 1) * F + 1:F]
                    act.activation(dst, oh_bank[g % 2][e][:, :].rearrange("p (t b) -> p t b", t=TILES),
                                   ACT.Copy).then_inc(s_lookup, 1)

            def quad_out(q):
                act.wait_ge(s_transposed, q + 1)
                t = q // QUADS_PER_TILE
                slot = q % QUADS_PER_TILE * QUAD
                dst = feat[:, t, 0:P * F].rearrange("p (b f) -> p f b", f=F)[:, slot:slot + QUAD, :]
                act.activation(dst, tr_bank[q % 2][:, :].rearrange("p (f b) -> p f b", f=QUAD),
                               ACT.Copy).then_inc(s_quad_in, 1)

            def gram_out(t):
                act.wait_ge(s_gram, 2 * t + 2)
                if t >= 2:
                    act.wait_ge(s_dump[t - 2], 16 * J)
                act.activation(gram_sb[:, t % 2, :, HALF:I],
                               gram_bank[1][:, 0:HALF * F].rearrange("p (i g) -> p g i", g=F),
                               ACT.Copy).then_inc(s_gram_b, 1)

            def mlp_out(t):
                act.wait_ge(s_l1, 2 * t + 1)
                for n in range(N_L1 // 2):
                    act.activation(h1_sb[:, t % 2, n, :], unit_ps(h1_bank, N_L1, n), ACT.Relu,
                                   bias=b1_sb[:, n:n + 1]).then_inc(s_h1_act, 1)
                act.wait_ge(s_l2, t + 1)
                act.activation(h2_sb[:, t % 2, 0, :], unit_ps(h2_bank, N_L2, 0), ACT.Relu,
                               bias=b2_sb[:, 0:1]).then_inc(s_h2_act, 1)
                act.wait_ge(s_l3, t + 1)
                act.activation(y_sb[:, t * P:(t + 1) * P], y_ps, ACT.Copy).then_inc(s_y, 1)

            for g in range(PAIRS):
                act.dma_start(ids_bc[:, g, :], ids_cols[g, :].partition_broadcast(OH_P)).then_inc(s_ids_bc[g], 16)
                if g == 1:
                    split_hi(0)
            act.dma_start(bottom_sb[:, :], bottom_t).then_inc(s_bottom, 16)
            act.wait_ge(s_bottom, 16)
            act.activation(feat[:, :, BOTTOM_SLOT:BOTTOM_SLOT + (P - 1) * F + 1:F],
                           bottom_sb[:, :].rearrange("p (t b) -> p t b", t=TILES), ACT.Copy).then_inc(s_bottom_in, 1)
            split_hi(1)
            act.dma_start(w1p_sb[0:Z_ROWS[0], :, :], w1_pairs).then_inc(s_weights, 16)
            act.dma_start(w1b_sb[:, :], w1_bottom).then_inc(s_weights, 16)
            act.dma_start(w2_sb[:, :, :], w2).then_inc(s_weights, 16)
            act.dma_start(w3_sb[:, :], w3).then_inc(s_weights, 16)
            act.dma_start(b1_sb[:, :], b1).then_inc(s_weights, 16)
            act.dma_start(b2_sb[:, :], b2).then_inc(s_weights, 16)
            for step, n in PLAN:
                if step == "lookup":
                    lookup_out(n)
                    if n + 2 < PAIRS:
                        split_hi(n + 2)
                elif step == "quad":
                    quad_out(n)
                elif step == "gram":
                    gram_out(n)
                else:
                    if n == 0:
                        act.wait_ge(s_weights, 16 * 6)
                    mlp_out(n)

        @block.vector
        def _(dve):
            def split_lo(g):
                dve.wait_ge(s_hi, g + 1)
                n = 2 * CHUNKS[g] * D
                dve.tensor_tensor(lo[:, g % 2, 0:n], raw[:, g % 2, 0:n], hi[:, g % 2, 0:n].bitcast(F32),
                                  ALU.subtract).then_inc(s_lo, 1)

            def make_one_hot(g, c):
                n = chunk_base[g] + c
                if c == 0:
                    dve.wait_ge(s_ids_bc[g], 16)
                if n >= OH_RING:
                    dve.wait_ge(s_one_hot_used, n - OH_RING + 1)
                dve.tensor_scalar(one_hot[:, n % OH_RING, :], ids_bc[:, g, :], row_no[CHUNKS[g]][:, c:c + 1],
                                  None, ALU.is_equal).then_inc(s_one_hot, 1)

            def gram_out(t):
                dve.wait_ge(s_gram, 2 * t + 1)
                if t >= 2:
                    dve.wait_ge(s_dump[t - 2], 16 * J)
                dve.tensor_copy(gram_sb[:, t % 2, :, 0:HALF],
                                gram_bank[0][:, 0:HALF * F].rearrange("p (i g) -> p g i", g=F)
                                ).then_inc(s_gram_a, 1)

            def mlp_out(t):
                dve.wait_ge(s_l1, 2 * t + 2)
                for n in range(N_L1 // 2, N_L1):
                    dve.tensor_scalar(h1_sb[:, t % 2, n, :], unit_ps(h1_bank, N_L1, n), b1_sb[:, n:n + 1], 0.0,
                                      ALU.add, ALU.max).then_inc(s_h1_dve, 1)
                dve.wait_ge(s_l2, t + 1)
                dve.tensor_scalar(h2_sb[:, t % 2, 1, :], unit_ps(h2_bank, N_L2, 1), b2_sb[:, 1:2], 0.0,
                                  ALU.add, ALU.max).then_inc(s_h2_dve, 1)

            dve.memset(feat[:, :, P * F:ET_ROW], 0.0).then_inc(s_pad, 1)
            dve.wait_ge(s_row_no, len(row_no))
            for g in range(PAIRS):
                for c in range(CHUNKS[g]):
                    make_one_hot(g, c)
                    if g == 0 and c == 1:
                        split_lo(0)
                    if c == 4 and g + 1 < PAIRS:
                        split_lo(g + 1)
            for step, n in PLAN:
                if step == "gram":
                    gram_out(n)
                elif step == "mlp":
                    if n == 0:
                        dve.wait_ge(s_weights, 16 * 6)
                    mlp_out(n)


PLAN = ([("lookup", 0), ("quad", 0), ("quad", 1), ("lookup", 1), ("quad", 2), ("quad", 3),
         ("lookup", 2), ("quad", 4), ("quad", 5), ("lookup", 3), ("quad", 6), ("quad", 7),
         ("lookup", 4), ("gram", 0), ("quad", 8), ("gram", 1), ("quad", 9), ("mlp", 0), ("quad", 10), ("mlp", 1),
         ("quad", 11), ("gram", 2), ("quad", 12), ("quad", 13), ("mlp", 2), ("quad", 14), ("quad", 15),
         ("gram", 3), ("mlp", 3)])


def pair_row(a, b):
    a, b = min(a, b), max(a, b)
    return a * F - a * (a + 1) // 2 + b - a - 1


def kernel(**inputs):
    import numpy as np
    import concourse.bacc as bacc
    from concourse.bass_utils import run_bass_kernel_spmd

    ids, w1 = np.asarray(inputs["ids"]), np.asarray(inputs["W_top1"])
    n_pairs = F * (F - 1) // 2
    w1_pairs = np.zeros((Z_ROWS[0], Z_CHUNKS, H1), w1.dtype)
    seen = set()
    for f in range(F - 1):
        for k in range(1, K_STEPS + 1):
            a, b = (f, f + k) if f + k < F else (f + 1, f + k - F)
            row = pair_row(SLOT_FEATURE[a], SLOT_FEATURE[b])
            if row not in seen:
                seen.add(row)
                w1_pairs[f % F_PER_CHUNK * K_STEPS + k - 1, f // F_PER_CHUNK] = w1[row]
    assert len(seen) == n_pairs

    def by_partition(x):
        x = np.asarray(x)
        return np.ascontiguousarray(x.reshape(x.shape[0] // P, P, -1).swapaxes(0, 1)).reshape(P, -1)

    arrays = {
        "ids_rows": by_partition(ids[:, GATHERED]),
        "ids_cols": np.ascontiguousarray(ids[:, ONE_HOT].T).reshape(PAIRS, 2 * B),
        "bottom_t": np.ascontiguousarray(np.asarray(inputs["r_bottom_output"]).T),
        "w1_pairs": w1_pairs,
        "w1_bottom": np.ascontiguousarray(w1[n_pairs:]),
        "b1": by_partition(inputs["b_top1"]),
        "w2": by_partition(inputs["W_top2"]).reshape(P, H1 // P, H2),
        "b2": by_partition(inputs["b_top2"]),
        "w3": by_partition(inputs["W_top3"]),
    }
    for f in range(F - 1):
        arrays[f"tbl_{f}"] = np.ascontiguousarray(inputs[f"tbl_{f}"])

    nc = bacc.Bacc("TRN2", target_bir_lowering=False, num_devices=1)
    aps = {name: nc.dram_tensor(name, a.shape, mybir.dt.from_np(a.dtype), kind="ExternalInput").ap()
           for name, a in arrays.items()}
    out = nc.dram_tensor("y", (B, 1), F32, kind="ExternalOutput").ap()
    tables = [aps[f"tbl_{f}"] for f in range(F - 1)]
    program(nc, aps["ids_rows"], aps["ids_cols"], tables, aps["bottom_t"], aps["w1_pairs"], aps["w1_bottom"],
            aps["b1"], aps["w2"], aps["b2"], aps["w3"], out)
    return run_bass_kernel_spmd(nc, [arrays], core_ids=[0]).results[0]["y"]
```

```python
from contextlib import ExitStack

import concourse.bass as bass
from concourse import mybir

F32 = mybir.dt.float32
F32R = mybir.dt.float32r
I32 = mybir.dt.int32
ACT = mybir.ActivationFunctionType
ALU = mybir.AluOpType

P = 128
D = 128
B = 512
TILES = B // P
F = 27
H1, H2 = 512, 256
TABLE_ROWS = [125000, 1250, 1000, 12500, 1250, 12500, 1000, 12500, 1250, 12500, 1250, 12500, 1250,
              1250, 1000, 1000, 1000, 12500, 1000, 1250, 12500, 1250, 12500, 1000, 1250, 1000]

ONE_HOT_GROUPS = [(2, 6), (14, 15), (16, 18), (23, 25)]
OH_P = 125
ONE_HOT = [f for group in ONE_HOT_GROUPS for f in group]
CHUNKS = [TABLE_ROWS[group[0]] // OH_P for group in ONE_HOT_GROUPS]
GROUPS = len(ONE_HOT_GROUPS)
MAX_CHUNKS = max(CHUNKS)
CHUNK_BASE = [sum(CHUNKS[:g]) for g in range(GROUPS + 1)]
MAX_COLS = max(len(group) * m * 128 for group, m in zip(ONE_HOT_GROUPS, CHUNKS))
PIECES = 2
WARM_UP = 16
OH_RING = 4
GATHERED = [f for f in range(F - 1) if f not in ONE_HOT]

N_GATHERED = len(GATHERED)
BATCHES = -(-N_GATHERED // 4)
BATCH_SLOTS = [range(N_GATHERED * n // BATCHES, N_GATHERED * (n + 1) // BATCHES) for n in range(BATCHES)]
SLOT_FEATURE = [f + 1 for f in GATHERED] + [f + 1 for f in ONE_HOT] + [0]
BOTTOM_SLOT = F - 1

SIDE = 4
SLOTS = 32
PER_BANK = 16
GRAM_BANKS = P // PER_BANK
GRAM_RING = 4
DUMPS = 2

K_STEPS = 14
F_PER_CHUNK = 9
Z_CHUNKS = 3
Z_FS = [9, 9, 8]
Z_ROWS = [n * K_STEPS for n in Z_FS]


def program(nc, ids_rows, ids_cols, tables, bottom_t, w1_pairs, w1_bottom, b1, w2, b2, w3, out):
    dump = nc.dram_tensor("gram_dump", (TILES, SLOTS, F, P), F32, kind="Internal").ap()

    ctx = ExitStack()
    with ctx:
        def sb(name, shape, dt=F32):
            return ctx.enter_context(nc.sbuf_tensor(name, shape, dt))

        def sem(name):
            return ctx.enter_context(nc.semaphore(name))

        ids_sb = sb("ids_sb", [P, TILES * len(GATHERED)], I32)
        rows_sb = sb("rows_sb", [P, 2, len(GATHERED), D])
        ident = sb("ident", [P, P])
        feat = sb("feat", [P, TILES, P, SLOTS])
        raw = sb("raw", [OH_P, 2, MAX_COLS])
        hi = sb("hi", [OH_P, 2, MAX_COLS], F32R)
        lo = sb("lo", [OH_P, 2, MAX_COLS], F32R)
        ids_bc = sb("ids_bc", [OH_P, len(ONE_HOT) * B], I32)
        row_no = {m: sb(f"row_no_{m}", [OH_P, m]) for m in sorted(set(CHUNKS))}
        one_hot = sb("one_hot", [OH_P, OH_RING, 2 * B], F32R)
        bottom_sb = sb("bottom_sb", [P, B])
        gram_sb = sb("gram_sb", [P, F, P])
        z = sb("z", [P, 2, Z_CHUNKS, P])
        w1p_sb = sb("w1p_sb", [P, Z_CHUNKS, H1])
        w1b_sb = sb("w1b_sb", [P, H1])
        w2_sb = sb("w2_sb", [P, H1 // P, H2])
        w3_sb = sb("w3_sb", [P, H2 // P])
        b1_sb = sb("b1_sb", [P, H1 // P])
        b2_sb = sb("b2_sb", [P, H2 // P])
        h1_sb = sb("h1_sb", [P, 2, H1 // P, P])
        h2_sb = sb("h2_sb", [P, 2, H2 // P, P])
        y_sb = sb("y_sb", [1, B])

        bank = [ctx.enter_context(nc.psum_tensor(f"bank{i}", [P, 512], F32)) for i in range(8)]
        oh_bank = [[bank[0], bank[1]], [bank[2], bank[3]]]
        gram_bank = bank[0:GRAM_RING]
        tr_bank = [bank[4], bank[5]]
        mlp_bank = [bank[6], bank[7]]
        y_ps = bank[6][0:1, 256:256 + P]

        s_ids = sem("s_ids")
        s_rows = [sem(f"s_rows{q}") for q in range(TILES * BATCHES)]
        s_raw = [[sem(f"s_raw{i}_{h}") for h in range(PIECES)] for i in range(2)]
        s_ids_bc = [sem(f"s_ids_bc{g}") for g in range(GROUPS)]
        s_weights = sem("s_weights")
        s_bottom = sem("s_bottom")
        s_row_no = sem("s_row_no")
        s_ident = sem("s_ident")
        s_pad = sem("s_pad")
        s_hi = sem("s_hi")
        s_lo = sem("s_lo")
        s_one_hot = sem("s_one_hot")
        s_one_hot_used = sem("s_one_hot_used")
        s_lookup = sem("s_lookup")
        s_bottom_in = sem("s_bottom_in")
        s_transposed = sem("s_transposed")
        s_batch_in = sem("s_batch_in")
        s_gram = sem("s_gram")
        s_gram_dve = sem("s_gram_dve")
        s_gram_act = sem("s_gram_act")
        s_dump = [sem(f"s_dump{t}") for t in range(TILES)]
        s_z = [sem(f"s_z{t}") for t in range(TILES)]
        s_l1 = sem("s_l1")
        s_h1_act = sem("s_h1_act")
        s_h1_dve = sem("s_h1_dve")
        s_l2 = sem("s_l2")
        s_h2_act = sem("s_h2_act")
        s_h2_dve = sem("s_h2_dve")
        s_l3 = sem("s_l3")
        s_y = sem("s_y")
        s_out = sem("s_out")

        block = ctx.enter_context(nc.Block())
        N_L1, N_L2 = H1 // P, H2 // P

        def unit_ps(n_units, n):
            half, nth = divmod(n, n_units // 2)
            return mlp_bank[half][:, nth * P:(nth + 1) * P]

        def piece(t, g, h):
            m, tabs = CHUNKS[g], len(ONE_HOT_GROUPS[g])
            a, b = m * h // PIECES, m * (h + 1) // PIECES
            return t[:, g % 2, 0:tabs * m * D].rearrange("p (e c) -> p e c", e=tabs)[:, :, a * D:b * D]

        def gram_block(u, j):
            src = gram_bank[u % GRAM_RING][j * SLOTS:(j + 1) * SLOTS, 0:SIDE * SIDE * F]
            src = src.rearrange("p (n k g) -> p k g n", n=SIDE, k=SIDE)[:, j, :, :]
            t, b = u // GRAM_BANKS, u % GRAM_BANKS * PER_BANK
            dst = gram_sb[t * SLOTS:(t + 1) * SLOTS, :, b:b + PER_BANK].rearrange("p g (n k) -> p k g n", k=SIDE)[:, j, :, :]
            return src, dst

        @block.sync
        def _(sp):
            sp.dma_start(ids_sb[:, :], ids_rows).then_inc(s_ids, 16)
            for g, group in enumerate(ONE_HOT_GROUPS):
                if g >= 2:
                    sp.wait_ge(s_lo, PIECES * (g - 1))
                m = CHUNKS[g]
                for h in range(PIECES):
                    for e, f in enumerate(group):
                        a, b = m * h // PIECES, m * (h + 1) // PIECES
                        src = tables[f].rearrange("(p c) d -> p c d", c=m)[:, a:b, :]
                        dst = piece(raw, g, h)[:, e, :].rearrange("p (c d) -> p c d", d=D)
                        sp.dma_start(dst, src).then_inc(s_raw[g % 2][h], 16)
            sp.dma_start(w1p_sb[0:Z_ROWS[0], :, :], w1_pairs).then_inc(s_weights, 16)
            sp.dma_start(w1b_sb[:, :], w1_bottom).then_inc(s_weights, 16)
            sp.dma_start(w2_sb[:, :, :], w2).then_inc(s_weights, 16)
            sp.dma_start(w3_sb[:, :], w3).then_inc(s_weights, 16)
            sp.dma_start(b1_sb[:, :], b1).then_inc(s_weights, 16)
            sp.dma_start(b2_sb[:, :], b2).then_inc(s_weights, 16)
            for t in range(TILES):
                for h in range(DUMPS):
                    fills = GRAM_BANKS * t + GRAM_BANKS * (h + 1) // DUMPS
                    sp.wait_ge(s_gram_dve, fills // 2)
                    sp.wait_ge(s_gram_act, fills // 2)
                    cols = slice(P * h // DUMPS, P * (h + 1) // DUMPS)
                    sp.dma_start(dump[t, :, :, cols], gram_sb[t * SLOTS:(t + 1) * SLOTS, :, cols]).then_inc(s_dump[t], 16)
                sp.wait_ge(s_dump[t], 16 * DUMPS)
                if t >= 2:
                    sp.wait_ge(s_l1, 2 * (t - 1))
                for c in range(Z_CHUNKS):
                    src = bass.AP(dump.tensor, t * SLOTS * F * P + c * F_PER_CHUNK * (F + 1) * P + P,
                                  [[(F + 1) * P, Z_FS[c]], [P, K_STEPS], [1, P]])
                    sp.dma_start(z[0:Z_ROWS[c], t % 2, c, :], src).then_inc(s_z[t], 16)
            sp.wait_ge(s_y, TILES)
            sp.dma_start(out.rearrange("(a b) n -> a (b n)", a=1), y_sb[:, :]).then_inc(s_out, 16)
            sp.wait_ge(s_out, 16)

        @block.gpsimd
        def _(pool):
            pool.memset(ident[:, :], 0.0).then_inc(s_ident, 1)
            for m in row_no:
                pool.iota(row_no[m][:, :], pattern=[[1, m]], base=0, channel_multiplier=m,
                          allow_small_or_imprecise_dtypes=True).then_inc(s_row_no, 1)
            pool.wait_ge(s_ident, 1)
            pool.affine_select(out=ident[:, :], in_=ident[:, :], compare_op=ALU.not_equal, fill=1.0,
                               base=0, pattern=[[-1, P]], channel_multiplier=1).then_inc(s_ident, 1)
            pool.wait_ge(s_ids, 16)
            for q in range(TILES * BATCHES):
                t, n = divmod(q, BATCHES)
                if t >= 2:
                    pool.wait_ge(s_transposed, q - 2 * BATCHES + 1)
                for s in BATCH_SLOTS[n]:
                    at = t * N_GATHERED + s
                    pool.indirect_dma_start(
                        out=rows_sb[:, t % 2, s, :], out_offset=None, in_=tables[GATHERED[s]][:, :],
                        in_offset=bass.IndirectOffsetOnAxis(ap=ids_sb[:, at:at + 1], axis=0),
                    ).then_inc(s_rows[q], 16)

        @block.tensor
        def _(pe):
            def lookup(g):
                if g >= 2:
                    pe.wait_ge(s_lookup, g - 1)
                m = CHUNKS[g]
                for c in range(m):
                    for h in range(PIECES):
                        if c == m * h // PIECES:
                            pe.wait_ge(s_lo, PIECES * g + h + 1)
                    pe.wait_ge(s_one_hot, CHUNK_BASE[g] + c + 1)
                    for e in range(len(ONE_HOT_GROUPS[g])):
                        col = (e * m + c) * D
                        for part in (hi, lo):
                            last = pe.matmul(oh_bank[g % 2][e][:, :], lhsT=part[:, g % 2, col:col + D],
                                             rhs=one_hot[:, (CHUNK_BASE[g] + c) % OH_RING, e * B:(e + 1) * B],
                                             start=(c == 0 and part is hi), stop=(c == m - 1 and part is lo))
                    last.then_inc(s_one_hot_used, 1)

            def transpose(q):
                t, n = divmod(q, BATCHES)
                pe.wait_ge(s_rows[q], 16 * len(BATCH_SLOTS[n]))
                if q >= 2:
                    pe.wait_ge(s_batch_in, q - 1)
                for k, s in enumerate(BATCH_SLOTS[n]):
                    last = pe.transpose(tr_bank[q % 2][:, k * P:(k + 1) * P], rows_sb[:, t % 2, s, :], ident[:, :])
                last.then_inc(s_transposed, 1)

            def gram(t):
                pe.wait_ge(s_batch_in, BATCHES * (t + 1))
                pe.wait_ge(s_lookup, GROUPS)
                pe.wait_ge(s_bottom_in, 1)
                pe.wait_ge(s_pad, 1)
                for u in range(GRAM_BANKS * t, GRAM_BANKS * (t + 1)):
                    if u >= GRAM_RING:
                        pe.wait_ge(s_gram_act if u % 2 else s_gram_dve, (u - GRAM_RING) // 2 + 1)
                    for n in range(SIDE):
                        at = u % GRAM_BANKS * PER_BANK + n * SIDE
                        samples = feat[:, t, at:at + SIDE, :].rearrange("p b f -> p (b f)")
                        last = pe.matmul(gram_bank[u % GRAM_RING][:, n * SIDE * F:(n + 1) * SIDE * F],
                                         lhsT=samples, rhs=feat[:, t, at:at + SIDE, 0:F], start=True, stop=True)
                    last.then_inc(s_gram, 1)

            def layer_1(t):
                if t == 0:
                    pe.wait_ge(s_weights, 16 * 6)
                    pe.wait_ge(s_bottom, 16)
                else:
                    pe.wait_ge(s_h2_dve, t)
                    pe.wait_ge(s_y, t)
                for n in range(N_L1):
                    pe.matmul(unit_ps(N_L1, n), lhsT=w1b_sb[:, n * P:(n + 1) * P],
                              rhs=bottom_sb[:, t * P:(t + 1) * P], start=(n % (N_L1 // 2) == 0), stop=False,
                              skip_group_check=True)
                pe.wait_ge(s_z[t], 16 * Z_CHUNKS)
                for n in range(N_L1):
                    for c in range(Z_CHUNKS):
                        k = Z_ROWS[c]
                        last = pe.matmul(unit_ps(N_L1, n), lhsT=w1p_sb[0:k, c, n * P:(n + 1) * P],
                                         rhs=z[0:k, t % 2, c, :], start=False, stop=(c == Z_CHUNKS - 1),
                                         skip_group_check=True)
                    if n % (N_L1 // 2) == N_L1 // 2 - 1:
                        last.then_inc(s_l1, 1)

            def layer_2(t):
                pe.wait_ge(s_h1_act, N_L1 // 2 * (t + 1))
                pe.wait_ge(s_h1_dve, N_L1 // 2 * (t + 1))
                for n in range(N_L2):
                    for k in range(N_L1):
                        last = pe.matmul(unit_ps(N_L2, n), lhsT=w2_sb[:, k, n * P:(n + 1) * P],
                                         rhs=h1_sb[:, t % 2, k, :], start=(k == 0), stop=(k == N_L1 - 1))
                    last.then_inc(s_l2, 1)

            def layer_3(t):
                pe.wait_ge(s_h2_act, t + 1)
                pe.matmul(y_ps, lhsT=w3_sb[:, 0:1], rhs=h2_sb[:, t % 2, 0, :], start=True, stop=False)
                pe.wait_ge(s_h2_dve, t + 1)
                pe.matmul(y_ps, lhsT=w3_sb[:, 1:2], rhs=h2_sb[:, t % 2, 1, :], start=False,
                          stop=True).then_inc(s_l3, 1)

            pe.wait_ge(s_ident, 2)
            for _ in range(WARM_UP):
                pe.matmul(gram_bank[3][:, 0:P], lhsT=ident[:, :], rhs=ident[:, :], start=True, stop=True)
            steps = {"lookup": lookup, "batch": transpose, "gram": gram, "layer 1": layer_1,
                     "layer 2": layer_2, "layer 3": layer_3}
            for step, n in PLAN:
                steps[step](n)

        @block.scalar
        def _(act):
            def split_hi(g):
                if g >= 2:
                    act.wait_ge(s_one_hot_used, CHUNK_BASE[g - 1])
                for h in range(PIECES):
                    act.wait_ge(s_raw[g % 2][h], 16 * sum(len(ONE_HOT_GROUPS[i]) for i in range(g % 2, g + 1, 2)))
                    act.activation(piece(hi, g, h), piece(raw, g, h), ACT.Copy).then_inc(s_hi, 1)

            def lookup_out(g):
                act.wait_ge(s_one_hot_used, CHUNK_BASE[g + 1])
                for e, f in enumerate(ONE_HOT_GROUPS[g]):
                    slot = N_GATHERED + ONE_HOT.index(f)
                    last = act.activation(feat[:, :, :, slot],
                                          oh_bank[g % 2][e][:, :].rearrange("p (t b) -> p t b", t=TILES), ACT.Copy)
                last.then_inc(s_lookup, 1)

            def batch_out(q):
                act.wait_ge(s_transposed, q + 1)
                t, n = divmod(q, BATCHES)
                slots = BATCH_SLOTS[n]
                dst = feat[:, t, :, slots[0]:slots[-1] + 1].rearrange("p b f -> p f b")
                src = tr_bank[q % 2][:, 0:len(slots) * P].rearrange("p (f b) -> p f b", b=P)
                act.activation(dst, src, ACT.Copy).then_inc(s_batch_in, 1)

            def gram_out(t):
                for u in range(GRAM_BANKS * t + 1, GRAM_BANKS * (t + 1), 2):
                    act.wait_ge(s_gram, u + 1)
                    for j in range(SIDE):
                        src, dst = gram_block(u, j)
                        last = act.activation(dst, src, ACT.Copy)
                    last.then_inc(s_gram_act, 1)

            def layer_1_out(t):
                if t == 0:
                    act.wait_ge(s_weights, 16 * 6)
                act.wait_ge(s_l1, 2 * t + 1)
                for n in range(N_L1 // 2):
                    act.activation(h1_sb[:, t % 2, n, :], unit_ps(N_L1, n), ACT.Relu,
                                   bias=b1_sb[:, n:n + 1]).then_inc(s_h1_act, 1)

            def layer_2_out(t):
                act.wait_ge(s_l2, 2 * t + 1)
                act.activation(h2_sb[:, t % 2, 0, :], unit_ps(N_L2, 0), ACT.Relu,
                               bias=b2_sb[:, 0:1]).then_inc(s_h2_act, 1)

            def layer_3_out(t):
                act.wait_ge(s_l3, t + 1)
                act.activation(y_sb[:, t * P:(t + 1) * P], y_ps, ACT.Copy).then_inc(s_y, 1)

            def load_ids(g):
                first = ONE_HOT.index(ONE_HOT_GROUPS[g][0])
                cols = slice(first * B, (first + len(ONE_HOT_GROUPS[g])) * B)
                act.dma_start(ids_bc[:, cols], ids_cols[cols].partition_broadcast(OH_P)).then_inc(s_ids_bc[g], 16)

            load_ids(0)
            split_hi(0)
            load_ids(1)
            act.dma_start(bottom_sb[:, :], bottom_t).then_inc(s_bottom, 16)
            split_hi(1)
            act.wait_ge(s_bottom, 16)
            act.activation(feat[:, :, :, BOTTOM_SLOT],
                           bottom_sb[:, :].rearrange("p (t b) -> p t b", t=TILES), ACT.Copy).then_inc(s_bottom_in, 1)
            for g in range(2, GROUPS):
                load_ids(g)
            def lookup_out_and_split(g):
                lookup_out(g)
                if g + 2 < GROUPS:
                    split_hi(g + 2)

            steps = {"lookup": lookup_out_and_split, "batch": batch_out, "gram": gram_out, "layer 1": layer_1_out,
                     "layer 2": layer_2_out, "layer 3": layer_3_out}
            for step, n in PLAN:
                steps[step](n)

        @block.vector
        def _(dve):
            def split_lo(g, h):
                dve.wait_ge(s_hi, PIECES * g + h + 1)
                dve.tensor_tensor(piece(lo, g, h), piece(raw, g, h), piece(hi, g, h).bitcast(F32),
                                  ALU.subtract).then_inc(s_lo, 1)

            def make_one_hot(g, c):
                n = CHUNK_BASE[g] + c
                if c == 0:
                    dve.wait_ge(s_ids_bc[g], 16)
                if n >= OH_RING:
                    dve.wait_ge(s_one_hot_used, n - OH_RING + 1)
                first, cols = ONE_HOT.index(ONE_HOT_GROUPS[g][0]) * B, len(ONE_HOT_GROUPS[g]) * B
                dve.tensor_scalar(one_hot[:, n % OH_RING, 0:cols], ids_bc[:, first:first + cols],
                                  row_no[CHUNKS[g]][:, c:c + 1], None, ALU.is_equal).then_inc(s_one_hot, 1)

            def gram_out(t):
                for u in range(GRAM_BANKS * t, GRAM_BANKS * (t + 1), 2):
                    dve.wait_ge(s_gram, u + 1)
                    for j in range(SIDE):
                        src, dst = gram_block(u, j)
                        last = dve.tensor_copy(dst, src)
                    last.then_inc(s_gram_dve, 1)

            def layer_1_out(t):
                if t == 0:
                    dve.wait_ge(s_weights, 16 * 6)
                dve.wait_ge(s_l1, 2 * t + 2)
                for n in range(N_L1 // 2, N_L1):
                    dve.tensor_scalar(h1_sb[:, t % 2, n, :], unit_ps(N_L1, n), b1_sb[:, n:n + 1], 0.0,
                                      ALU.add, ALU.max).then_inc(s_h1_dve, 1)

            def layer_2_out(t):
                dve.wait_ge(s_l2, 2 * t + 2)
                dve.tensor_scalar(h2_sb[:, t % 2, 1, :], unit_ps(N_L2, 1), b2_sb[:, 1:2], 0.0,
                                  ALU.add, ALU.max).then_inc(s_h2_dve, 1)

            dve.memset(feat[:, :, :, F:SLOTS], 0.0).then_inc(s_pad, 1)
            dve.wait_ge(s_row_no, len(row_no))
            for g in range(GROUPS):
                for c in range(CHUNKS[g]):
                    make_one_hot(g, c)
                    if g == 0 and c in (1, 3):
                        split_lo(0, c // 2)
                    if g + 1 < GROUPS and c in (4, 6):
                        split_lo(g + 1, c // 2 - 2)
            steps = {"gram": gram_out, "layer 1": layer_1_out, "layer 2": layer_2_out}
            for step, n in PLAN:
                if step in steps:
                    steps[step](n)


def plan():
    def batches(a, b):
        return [("batch", q) for q in range(a, b)]

    n = BATCHES
    return ([("lookup", 0)] + batches(0, 2) + [("lookup", 1)] + batches(2, 4) + [("lookup", 2)] + batches(4, 6)
            + [("lookup", 3)] + batches(6, 8) + [("gram", 0)] + batches(8, 9) + batches(9, 2 * n)
            + [("gram", 1), ("layer 1", 0)] + batches(2 * n, 2 * n + 1)
            + [("layer 2", 0)] + batches(2 * n + 1, 2 * n + 2) + [("layer 3", 0)] + batches(2 * n + 2, 3 * n)
            + [("layer 1", 1), ("gram", 2), ("layer 2", 1)] + batches(3 * n, 3 * n + 1) + [("layer 3", 1)]
            + batches(3 * n + 1, 4 * n)
            + [("gram", 3), ("layer 1", 2), ("layer 2", 2), ("layer 3", 2),
               ("layer 1", 3), ("layer 2", 3), ("layer 3", 3)])


PLAN = plan()


def pair_row(a, b):
    a, b = min(a, b), max(a, b)
    return a * F - a * (a + 1) // 2 + b - a - 1


def kernel(**inputs):
    import numpy as np
    import concourse.bacc as bacc
    from concourse.bass_utils import run_bass_kernel_spmd

    ids, w1 = np.asarray(inputs["ids"]), np.asarray(inputs["W_top1"])
    n_pairs = F * (F - 1) // 2
    w1_pairs = np.zeros((Z_ROWS[0], Z_CHUNKS, H1), w1.dtype)
    seen = set()
    for f in range(F - 1):
        for k in range(1, K_STEPS + 1):
            a, b = (f, f + k) if f + k < F else (f + 1, f + k - F)
            row = pair_row(SLOT_FEATURE[a], SLOT_FEATURE[b])
            if row not in seen:
                seen.add(row)
                w1_pairs[f % F_PER_CHUNK * K_STEPS + k - 1, f // F_PER_CHUNK] = w1[row]
    assert len(seen) == n_pairs

    def by_partition(x):
        x = np.asarray(x)
        return np.ascontiguousarray(x.reshape(x.shape[0] // P, P, -1).swapaxes(0, 1)).reshape(P, -1)

    arrays = {
        "ids_rows": by_partition(ids[:, GATHERED]),
        "ids_cols": np.ascontiguousarray(ids[:, ONE_HOT].T).reshape(-1),
        "bottom_t": np.ascontiguousarray(np.asarray(inputs["r_bottom_output"]).T),
        "w1_pairs": w1_pairs,
        "w1_bottom": np.ascontiguousarray(w1[n_pairs:]),
        "b1": by_partition(inputs["b_top1"]),
        "w2": by_partition(inputs["W_top2"]).reshape(P, H1 // P, H2),
        "b2": by_partition(inputs["b_top2"]),
        "w3": by_partition(inputs["W_top3"]),
    }
    for f in range(F - 1):
        arrays[f"tbl_{f}"] = np.ascontiguousarray(inputs[f"tbl_{f}"])

    nc = bacc.Bacc("TRN2", target_bir_lowering=False, num_devices=1)
    aps = {name: nc.dram_tensor(name, a.shape, mybir.dt.from_np(a.dtype), kind="ExternalInput").ap()
           for name, a in arrays.items()}
    out = nc.dram_tensor("y", (B, 1), F32, kind="ExternalOutput").ap()
    tables = [aps[f"tbl_{f}"] for f in range(F - 1)]
    program(nc, aps["ids_rows"], aps["ids_cols"], tables, aps["bottom_t"], aps["w1_pairs"], aps["w1_bottom"],
            aps["b1"], aps["w2"], aps["b2"], aps["w3"], out)
    return run_bass_kernel_spmd(nc, [arrays], core_ids=[0]).results[0]["y"]
```

```python
from contextlib import ExitStack

import concourse.bass as bass
from concourse import mybir

F32 = mybir.dt.float32
F32R = mybir.dt.float32r
I32 = mybir.dt.int32
ACT = mybir.ActivationFunctionType
ALU = mybir.AluOpType

P = 128
D = 128
B = 512
TILES = B // P
F = 27
H1, H2 = 512, 256
TABLE_ROWS = [125000, 1250, 1000, 12500, 1250, 12500, 1000, 12500, 1250, 12500, 1250, 12500, 1250,
              1250, 1000, 1000, 1000, 12500, 1000, 1250, 12500, 1250, 12500, 1000, 1250, 1000]

ONE_HOT_GROUPS = [(2, 6), (14, 15), (16, 18), (23, 25), (24,), (21,)]
OH_P = 125
ONE_HOT = [f for group in ONE_HOT_GROUPS for f in group]
FROM_TILE = {21: 1}
CHUNKS = [TABLE_ROWS[group[0]] // OH_P for group in ONE_HOT_GROUPS]
GROUPS = len(ONE_HOT_GROUPS)
LATE_GROUP = GROUPS - 1
CHUNK_BASE = [sum(CHUNKS[:g]) for g in range(GROUPS + 1)]
MAX_COLS = max(len(group) * m * 128 for group, m in zip(ONE_HOT_GROUPS, CHUNKS))
BOUNDS = [[0, 2, 5, 8]] + [[0, m // 2, m] for m in CHUNKS[1:]]
PIECES = [len(bounds) - 1 for bounds in BOUNDS]
PIECES_TO = [sum(PIECES[:g]) for g in range(GROUPS + 1)]
WARM_UP = 11
OH_RING = 4
GATHERED = [f for f in range(F - 1) if f not in ONE_HOT] + list(FROM_TILE)

N_GATHERED = [len(GATHERED) - sum(start <= t for start in FROM_TILE.values()) for t in range(TILES)]
BATCH_STARTS = [list(range(0, n, 4)) for n in N_GATHERED]
BATCH_STARTS[-1].append(N_GATHERED[-1] - 2)
BATCHES = [(t, range(a, b)) for t, starts in enumerate(BATCH_STARTS)
           for a, b in zip(starts, starts[1:] + [N_GATHERED[t]])]
BATCHES_TO = [sum(batch[0] < t for batch in BATCHES) for t in range(TILES + 1)]
SLOT_TABLE = GATHERED + [f for f in ONE_HOT if f not in FROM_TILE]
SLOT_FEATURE = [f + 1 for f in SLOT_TABLE] + [0]
BOTTOM_SLOT = F - 1
LAST = TILES - 1

SLOTS = 32
LANES = P // SLOTS
FILLS = [(0, 0, 16), (0, 64, 16), (1, 0, 16), (1, 64, 16), (2, 0, 16), (2, 64, 16),
         (3, 0, 16), (3, 64, 12), (3, 112, 4)]
FILLS_TO = [sum(fill[0] < t for fill in FILLS) for t in range(TILES + 1)]
GRAM_RING = 2

K_STEPS = 14
F_PER_CHUNK = 9
Z_CHUNKS = 3
Z_FS = [9, 9, 8]
Z_ROWS = [n * K_STEPS for n in Z_FS]


def program(nc, ids_rows, ids_cols, tables, bottom_t, w1_pairs, w1_bottom, b1, w2, b2, w3, out):
    dump = nc.dram_tensor("gram_dump", (TILES, SLOTS, F, P), F32, kind="Internal").ap()

    ctx = ExitStack()
    with ctx:
        def sb(name, shape, dt=F32):
            return ctx.enter_context(nc.sbuf_tensor(name, shape, dt))

        def sem(name):
            return ctx.enter_context(nc.semaphore(name))

        ids_sb = sb("ids_sb", [P, TILES * len(GATHERED)], I32)
        rows_sb = sb("rows_sb", [P, 2, len(GATHERED), D])
        ident = sb("ident", [P, P])
        feat = sb("feat", [P, TILES, P, F])
        raw = sb("raw", [OH_P, 2, MAX_COLS])
        hi = sb("hi", [OH_P, 2, MAX_COLS], F32R)
        lo = sb("lo", [OH_P, 2, MAX_COLS], F32R)
        ids_bc = sb("ids_bc", [OH_P, len(ONE_HOT) * B], I32)
        row_no = {m: sb(f"row_no_{m}", [OH_P, m]) for m in sorted(set(CHUNKS))}
        one_hot = sb("one_hot", [OH_P, OH_RING, 2 * B], F32R)
        bottom_sb = sb("bottom_sb", [P, B])
        gram_sb = sb("gram_sb", [P, F, P])
        z = sb("z", [P, 2, Z_CHUNKS, P])
        w1p_sb = sb("w1p_sb", [P, Z_CHUNKS, H1])
        w1b_sb = sb("w1b_sb", [P, H1])
        w2_sb = sb("w2_sb", [P, H1 // P, H2])
        b2_bc = sb("b2_bc", [P, H2])
        w3_bc = sb("w3_bc", [P, H2])
        b1_sb = sb("b1_sb", [P, H1 // P])
        h1_sb = sb("h1_sb", [P, 2, H1 // P, P])
        pre2_sb = sb("pre2_sb", [P, H2])
        terms_sb = sb("terms_sb", [P, H2])
        y_sb = sb("y_sb", [P, TILES])

        bank = [ctx.enter_context(nc.psum_tensor(f"bank{i}", [P, 512], F32)) for i in range(8)]
        oh_bank = [[bank[0], bank[1]], [bank[2], bank[3]]]
        gram_bank = bank[0:GRAM_RING]
        tr_bank = [bank[4], bank[5]]
        mlp_bank = [[bank[6], bank[7]], [bank[2], bank[3]]]

        s_ids = sem("s_ids")
        s_rows = [sem(f"s_rows{q}") for q in range(len(BATCHES))]
        s_raw = [[sem(f"s_raw{i}_{h}") for h in range(max(PIECES))] for i in range(2)]
        s_ids_bc = [sem(f"s_ids_bc{g}") for g in range(GROUPS)]
        s_weights = sem("s_weights")
        s_bottom = sem("s_bottom")
        s_row_no = sem("s_row_no")
        s_ident = sem("s_ident")
        s_hi = sem("s_hi")
        s_lo = sem("s_lo")
        s_one_hot = sem("s_one_hot")
        s_one_hot_used = sem("s_one_hot_used")
        s_lookup = sem("s_lookup")
        s_bottom_in = sem("s_bottom_in")
        s_transposed = sem("s_transposed")
        s_batch_in = sem("s_batch_in")
        s_gram = sem("s_gram")
        s_gram_dve = sem("s_gram_dve")
        s_gram_act = sem("s_gram_act")
        s_dump = [[sem(f"s_dump{t}_{h}") for h in range(2)] for t in range(TILES)]
        s_z = [[sem(f"s_z{t}_{c}") for c in range(Z_CHUNKS)] for t in range(TILES)]
        s_l1 = sem("s_l1")
        s_h1_act = sem("s_h1_act")
        s_h1_dve = sem("s_h1_dve")
        s_l2 = sem("s_l2")
        s_pre2 = sem("s_pre2")
        s_y = sem("s_y")
        s_out = sem("s_out")

        block = ctx.enter_context(nc.Block())
        N_L1 = H1 // P

        def l1_ps(t, n):
            if t == LAST:
                return bank[n][:, 0:P]
            half, nth = divmod(n, N_L1 // 2)
            return mlp_bank[t % 2][half][:, nth * P:(nth + 1) * P]

        def l1_opens(t, n):
            return t == LAST or n % (N_L1 // 2) == 0

        def l1_done(t, n):
            return N_L1 * t + (n + 1 if t == LAST else (n // (N_L1 // 2) + 1) * (N_L1 // 2))

        def l2_ps(t):
            return (tr_bank[0] if t == LAST else mlp_bank[t % 2][0])[:, 0:H2]

        def piece(t, g, h):
            m, tabs = CHUNKS[g], len(ONE_HOT_GROUPS[g])
            a, b = BOUNDS[g][h:h + 2]
            return t[:, g % 2, 0:tabs * m * D].rearrange("p (e c) -> p e c", e=tabs)[:, :, a * D:b * D]

        def one_hots(g, c, e=0, tabs=1):
            if g != LATE_GROUP:
                return one_hot[:, (CHUNK_BASE[g] + c) % OH_RING, e * B:(e + tabs) * B]
            n = B - FROM_TILE[ONE_HOT_GROUPS[g][0]] * P
            return one_hot[:, :, :].rearrange("p r b -> p (r b)")[:, c * n:(c + 1) * n]

        def gram_block(u, j):
            t, first, n = FILLS[u]
            src = gram_bank[u % GRAM_RING][j * SLOTS:(j + 1) * SLOTS, 0:n * F]
            return (src.rearrange("p (n g) -> p g n", g=F),
                    gram_sb[t * SLOTS:(t + 1) * SLOTS, :, first + n * j:first + n * (j + 1)])

        @block.sync
        def _(sp):
            sp.dma_start(ids_sb[:, :], ids_rows).then_inc(s_ids, 16)
            for g, group in enumerate(ONE_HOT_GROUPS):
                if g >= 2:
                    sp.wait_ge(s_lo, PIECES_TO[g - 1])
                m = CHUNKS[g]
                for h in range(PIECES[g]):
                    for e, f in enumerate(group):
                        a, b = BOUNDS[g][h:h + 2]
                        src = tables[f].rearrange("(p c) d -> p c d", c=m)[:, a:b, :]
                        dst = piece(raw, g, h)[:, e, :].rearrange("p (c d) -> p c d", d=D)
                        sp.dma_start(dst, src).then_inc(s_raw[g % 2][h], 16)
            sp.dma_start(w1p_sb[0:Z_ROWS[0], :, :], w1_pairs).then_inc(s_weights, 16)
            sp.dma_start(w1b_sb[:, :], w1_bottom).then_inc(s_weights, 16)
            sp.dma_start(w2_sb[:, :, :], w2).then_inc(s_weights, 16)
            sp.dma_start(w3_bc[:, :], w3.partition_broadcast(P)).then_inc(s_weights, 16)
            sp.dma_start(b1_sb[:, :], b1).then_inc(s_weights, 16)
            sp.dma_start(b2_bc[:, :], b2.partition_broadcast(P)).then_inc(s_weights, 16)
            for t in range(TILES):
                sp.wait_ge(s_gram_dve, FILLS_TO[t + 1])
                sp.wait_ge(s_gram_act, FILLS_TO[t + 1])
                for h in range(2):
                    slots = slice(h * SLOTS // 2, (h + 1) * SLOTS // 2)
                    src = gram_sb[t * SLOTS + slots.start:t * SLOTS + slots.stop, :, :]
                    sp.dma_start(dump[t, slots, :, :], src).then_inc(s_dump[t][h], 16)
                if t >= 2:
                    sp.wait_ge(s_l1, N_L1 * (t - 1))
                for c in range(Z_CHUNKS):
                    if c < 2:
                        sp.wait_ge(s_dump[t][c], 16)
                    src = bass.AP(dump.tensor, t * SLOTS * F * P + c * F_PER_CHUNK * (F + 1) * P + P,
                                  [[(F + 1) * P, Z_FS[c]], [P, K_STEPS], [1, P]])
                    sp.dma_start(z[0:Z_ROWS[c], t % 2, c, :], src).then_inc(s_z[t][c], 16)
            sp.wait_ge(s_y, TILES)
            sp.dma_start(out.rearrange("(p t) n -> p (t n)", t=TILES), y_sb[:, :]).then_inc(s_out, 16)
            sp.wait_ge(s_out, 16)

        @block.gpsimd
        def _(pool):
            pool.memset(ident[:, :], 0.0).then_inc(s_ident, 1)
            for m in row_no:
                pool.iota(row_no[m][:, :], pattern=[[1, m]], base=0, channel_multiplier=m,
                          allow_small_or_imprecise_dtypes=True).then_inc(s_row_no, 1)
            pool.wait_ge(s_ident, 1)
            pool.affine_select(out=ident[:, :], in_=ident[:, :], compare_op=ALU.not_equal, fill=1.0,
                               base=0, pattern=[[-1, P]], channel_multiplier=1).then_inc(s_ident, 1)
            pool.wait_ge(s_ids, 16)
            for q, (t, slots) in enumerate(BATCHES):
                if t >= 2:
                    pool.wait_ge(s_transposed, BATCHES_TO[t - 2] + q - BATCHES_TO[t] + 1)
                for s in slots:
                    at = t * len(GATHERED) + s
                    pool.indirect_dma_start(
                        out=rows_sb[:, t % 2, s, :], out_offset=None, in_=tables[GATHERED[s]][:, :],
                        in_offset=bass.IndirectOffsetOnAxis(ap=ids_sb[:, at:at + 1], axis=0),
                    ).then_inc(s_rows[q], 16)

        @block.tensor
        def _(pe):
            def lookup(g, piece):
                if g >= 2 and piece == 0:
                    pe.wait_ge(s_lookup, g - 1)
                m = CHUNKS[g]
                pe.wait_ge(s_lo, PIECES_TO[g] + piece + 1)
                for c in range(*BOUNDS[g][piece:piece + 2]):
                    pe.wait_ge(s_one_hot, CHUNK_BASE[g] + c + 1)
                    for e, f in enumerate(ONE_HOT_GROUPS[g]):
                        col, b = (e * m + c) * D, FROM_TILE.get(f, 0) * P
                        for part in (hi, lo):
                            last = pe.matmul(oh_bank[g % 2][e][:, b:], lhsT=part[:, g % 2, col:col + D],
                                             rhs=one_hots(g, c, e),
                                             start=(c == 0 and part is hi), stop=(c == m - 1 and part is lo))
                    last.then_inc(s_one_hot_used, 1)

            def transpose(q):
                t, slots = BATCHES[q]
                pe.wait_ge(s_rows[q], 16 * len(slots))
                if q >= 2:
                    pe.wait_ge(s_batch_in, q - 1)
                for k, s in enumerate(slots):
                    last = pe.transpose(tr_bank[q % 2][:, k * P:(k + 1) * P], rows_sb[:, t % 2, s, :], ident[:, :])
                last.then_inc(s_transposed, 1)

            def gram(u):
                t, first, n = FILLS[u]
                pe.wait_ge(s_batch_in, BATCHES_TO[t + 1])
                if u == 0:
                    pe.wait_ge(s_lookup, LATE_GROUP)
                    pe.wait_ge(s_bottom_in, 1)
                if u == FILLS_TO[FROM_TILE[ONE_HOT_GROUPS[LATE_GROUP][0]]]:
                    pe.wait_ge(s_lookup, LATE_GROUP + 1)
                if u >= GRAM_RING:
                    pe.wait_ge(s_gram_act, u - GRAM_RING + 1)
                    pe.wait_ge(s_gram_dve, u - GRAM_RING + 1)
                for i in range(n):
                    for j in range(LANES):
                        own = feat[:, t, first + n * j + i, :]
                        last = pe.matmul(gram_bank[u % GRAM_RING][j * SLOTS:j * SLOTS + F, i * F:(i + 1) * F],
                                         lhsT=own, rhs=own, start=True, stop=True, tile_position=(0, j * SLOTS))
                last.then_inc(s_gram, 1)

            def bottom_part(t):
                if t == 0:
                    pe.wait_ge(s_weights, 16 * 6)
                    pe.wait_ge(s_bottom, 16)
                elif t == 1:
                    pe.wait_ge(s_lookup, GROUPS)
                else:
                    pe.wait_ge(s_pre2, t - 1)
                    pe.wait_ge(s_h1_dve, N_L1 // 2 * (t - 1))
                if t == LAST:
                    pe.wait_ge(s_gram_act, FILLS_TO[TILES])
                    pe.wait_ge(s_gram_dve, FILLS_TO[TILES])
                for n in range(N_L1):
                    pe.matmul(l1_ps(t, n), lhsT=w1b_sb[:, n * P:(n + 1) * P], rhs=bottom_sb[:, t * P:(t + 1) * P],
                              start=l1_opens(t, n), stop=False, skip_group_check=True)

            def layer_1(t, c):
                pe.wait_ge(s_z[t][c], 16)
                k = Z_ROWS[c]
                for n in range(N_L1):
                    product = pe.matmul(l1_ps(t, n), lhsT=w1p_sb[0:k, c, n * P:(n + 1) * P],
                                        rhs=z[0:k, t % 2, c, :], start=False, stop=(c == Z_CHUNKS - 1),
                                        skip_group_check=True)
                    if c == Z_CHUNKS - 1:
                        product.then_inc(s_l1, 1)

            def layer_2(t):
                if t < LAST:
                    pe.wait_ge(s_h1_act, N_L1 // 2 * (t + 1))
                else:
                    pe.wait_ge(s_batch_in, len(BATCHES))
                for k in range(N_L1):
                    half, nth = divmod(k, N_L1 // 2)
                    pe.wait_ge(s_h1_dve if half else s_h1_act, N_L1 // 2 * t + nth + 1)
                    product = pe.matmul(l2_ps(t), lhsT=h1_sb[:, t % 2, k, :], rhs=w2_sb[:, k, :],
                                        start=(k == 0), stop=(k == N_L1 - 1))
                product.then_inc(s_l2, 1)

            pe.wait_ge(s_ident, 2)
            for _ in range(WARM_UP):
                pe.matmul(bank[3][:, 0:P], lhsT=ident[:, :], rhs=ident[:, :], start=True, stop=True)
            steps = {"lookup": lookup, "batch": transpose, "gram": gram, "bottom part": bottom_part,
                     "layer 1": layer_1, "layer 2": layer_2}
            for step, *n in PLAN:
                steps[step](*n)

        @block.scalar
        def _(act):
            def split_hi(g):
                if g >= 2:
                    act.wait_ge(s_one_hot_used, CHUNK_BASE[g - 1])
                for h in range(PIECES[g]):
                    act.wait_ge(s_raw[g % 2][h], 16 * sum(len(ONE_HOT_GROUPS[i]) for i in range(g % 2, g + 1, 2)
                                                          if h < PIECES[i]))
                    act.activation(piece(hi, g, h), piece(raw, g, h), ACT.Copy).then_inc(s_hi, 1)

            def lookup_out(g):
                act.wait_ge(s_one_hot_used, CHUNK_BASE[g + 1])
                for e, f in enumerate(ONE_HOT_GROUPS[g]):
                    t = FROM_TILE.get(f, 0)
                    last = act.activation(feat[:, t:, :, SLOT_TABLE.index(f)],
                                          oh_bank[g % 2][e][:, t * P:].rearrange("p (t b) -> p t b", b=P), ACT.Copy)
                last.then_inc(s_lookup, 1)

            def batch_out(q):
                act.wait_ge(s_transposed, q + 1)
                t, slots = BATCHES[q]
                dst = feat[:, t, :, slots[0]:slots[-1] + 1].rearrange("p b f -> p f b")
                src = tr_bank[q % 2][:, 0:len(slots) * P].rearrange("p (f b) -> p f b", b=P)
                act.activation(dst, src, ACT.Copy).then_inc(s_batch_in, 1)

            def gram_out(u):
                act.wait_ge(s_gram, u + 1)
                for j in (2, 3):
                    src, dst = gram_block(u, j)
                    last = act.activation(dst, src, ACT.Copy)
                last.then_inc(s_gram_act, 1)

            def layer_1_out(t, c):
                if c < Z_CHUNKS - 1:
                    return
                if t == 0:
                    act.wait_ge(s_weights, 16 * 6)
                for n in range(N_L1 // 2):
                    act.wait_ge(s_l1, l1_done(t, n))
                    act.activation(h1_sb[:, t % 2, n, :], l1_ps(t, n), ACT.Relu,
                                   bias=b1_sb[:, n:n + 1]).then_inc(s_h1_act, 1)

            def load_ids(g):
                first = ONE_HOT.index(ONE_HOT_GROUPS[g][0])
                start = FROM_TILE.get(ONE_HOT_GROUPS[g][0], 0) * P
                cols = slice(first * B + start, (first + len(ONE_HOT_GROUPS[g])) * B)
                act.dma_start(ids_bc[:, cols], ids_cols[cols].partition_broadcast(OH_P)).then_inc(s_ids_bc[g], 16)

            load_ids(0)
            split_hi(0)
            load_ids(1)
            act.dma_start(bottom_sb[:, :], bottom_t).then_inc(s_bottom, 16)
            split_hi(1)
            act.wait_ge(s_bottom, 16)
            act.activation(feat[:, :, :, BOTTOM_SLOT],
                           bottom_sb[:, :].rearrange("p (t b) -> p t b", t=TILES), ACT.Copy).then_inc(s_bottom_in, 1)
            for g in range(2, GROUPS):
                load_ids(g)

            def lookup_out_and_split(g, piece):
                if piece == PIECES[g] - 1:
                    lookup_out(g)
                    if g + 2 < GROUPS:
                        split_hi(g + 2)

            steps = {"lookup": lookup_out_and_split, "batch": batch_out, "gram": gram_out, "layer 1": layer_1_out}
            for step, *n in PLAN:
                if step in steps:
                    steps[step](*n)

        @block.vector
        def _(dve):
            def split_lo(g, h):
                dve.wait_ge(s_hi, PIECES_TO[g] + h + 1)
                dve.tensor_tensor(piece(lo, g, h), piece(raw, g, h), piece(hi, g, h).bitcast(F32),
                                  ALU.subtract).then_inc(s_lo, 1)

            def make_one_hot(g, c):
                n = CHUNK_BASE[g] + c
                if c == 0:
                    dve.wait_ge(s_ids_bc[g], 16)
                if g == LATE_GROUP and c == 0:
                    dve.wait_ge(s_one_hot_used, n)
                elif g != LATE_GROUP and n >= OH_RING:
                    dve.wait_ge(s_one_hot_used, n - OH_RING + 1)
                start = FROM_TILE.get(ONE_HOT_GROUPS[g][0], 0) * P
                first, tabs = ONE_HOT.index(ONE_HOT_GROUPS[g][0]) * B, len(ONE_HOT_GROUPS[g])
                dve.tensor_scalar(one_hots(g, c, 0, tabs), ids_bc[:, first + start:first + tabs * B],
                                  row_no[CHUNKS[g]][:, c:c + 1], None, ALU.is_equal).then_inc(s_one_hot, 1)

            def gram_out(u):
                dve.wait_ge(s_gram, u + 1)
                for j in (0, 1):
                    src, dst = gram_block(u, j)
                    last = dve.tensor_copy(dst, src)
                last.then_inc(s_gram_dve, 1)

            def layer_1_out(t, c):
                if c < Z_CHUNKS - 1:
                    return
                if t == 0:
                    dve.wait_ge(s_weights, 16 * 6)
                for n in range(N_L1 // 2, N_L1):
                    dve.wait_ge(s_l1, l1_done(t, n))
                    dve.tensor_scalar(h1_sb[:, t % 2, n, :], l1_ps(t, n), b1_sb[:, n:n + 1], 0.0,
                                      ALU.add, ALU.max).then_inc(s_h1_dve, 1)

            def layers_2_and_3(t):
                dve.wait_ge(s_l2, t + 1)
                if t > 0:
                    dve.wait_ge(s_y, t)
                dve.tensor_tensor(pre2_sb[:, :], l2_ps(t), b2_bc[:, :], ALU.add).then_inc(s_pre2, 1)
                dve.wait_ge(s_pre2, t + 1)
                dve.scalar_tensor_tensor(out=terms_sb[:, :], in0=pre2_sb[:, :], scalar=0.0, in1=w3_bc[:, :],
                                         op0=ALU.max, op1=ALU.mult, accum_out=y_sb[:, t:t + 1]).then_inc(s_y, 1)

            dve.wait_ge(s_row_no, len(row_no))
            for g in range(GROUPS):
                for c in range(CHUNKS[g]):
                    make_one_hot(g, c)
                    if g == 0 and c in (1, 2, 4):
                        split_lo(0, c // 2)
                    if g > 0 and c == 1:
                        split_lo(g, 1)
                    if g + 1 < GROUPS and c == CHUNKS[g] - 1:
                        split_lo(g + 1, 0)
            steps = {"gram": gram_out, "layer 1": layer_1_out, "layer 2": layers_2_and_3}
            for step, *n in PLAN:
                if step in steps:
                    steps[step](*n)


def plan():
    def batches(*qs):
        return [("batch", q) for q in qs]

    def fills(t, *us):
        return [("gram", FILLS_TO[t] + u) for u in us]

    def layer_1(t, *chunks):
        return [("layer 1", t, c) for c in chunks or range(Z_CHUNKS)]

    def lookup(g, *pieces):
        return [("lookup", g, h) for h in pieces or range(PIECES[g])]

    return (lookup(0, 0, 1) + batches(0) + lookup(0, 2) + batches(1) + lookup(1) + batches(2)
            + lookup(2, 0) + batches(3, 4) + lookup(2, 1) + batches(5) + lookup(3) + batches(6, 7)
            + lookup(4) + batches(8)
            + [("bottom part", 0)] + batches(9) + fills(0, 0, 1) + lookup(5) + batches(10, 11)
            + fills(1, 0) + [("bottom part", 1)] + batches(12) + fills(1, 1)
            + layer_1(0) + fills(2, 0) + [("layer 2", 0)] + batches(13) + fills(2, 1)
            + batches(14) + layer_1(1) + batches(15, 16) + [("layer 2", 1)] + batches(17)
            + fills(3, 0, 1, 2) + [("bottom part", 2)] + layer_1(2) + [("bottom part", 3), ("layer 2", 2)]
            + layer_1(3) + [("layer 2", 3)])


PLAN = plan()


def pair_row(a, b):
    a, b = min(a, b), max(a, b)
    return a * F - a * (a + 1) // 2 + b - a - 1


def kernel(**inputs):
    import numpy as np
    import concourse.bacc as bacc
    from concourse.bass_utils import run_bass_kernel_spmd

    ids, w1 = np.asarray(inputs["ids"]), np.asarray(inputs["W_top1"])
    n_pairs = F * (F - 1) // 2
    w1_pairs = np.zeros((Z_ROWS[0], Z_CHUNKS, H1), w1.dtype)
    seen = set()
    for f in range(F - 1):
        for k in range(1, K_STEPS + 1):
            a, b = (f, f + k) if f + k < F else (f + 1, f + k - F)
            row = pair_row(SLOT_FEATURE[a], SLOT_FEATURE[b])
            if row not in seen:
                seen.add(row)
                w1_pairs[f % F_PER_CHUNK * K_STEPS + k - 1, f // F_PER_CHUNK] = w1[row]
    assert len(seen) == n_pairs

    def by_partition(x):
        x = np.asarray(x)
        return np.ascontiguousarray(x.reshape(x.shape[0] // P, P, -1).swapaxes(0, 1)).reshape(P, -1)

    def by_tile(x):
        return np.ascontiguousarray(np.moveaxis(x.reshape(P, TILES, -1), 2, 0).swapaxes(1, 2)).reshape(-1, B)

    arrays = {
        "ids_rows": np.ascontiguousarray(ids[:, GATHERED]).reshape(P, -1),
        "ids_cols": by_tile(ids[:, ONE_HOT]).reshape(-1),
        "bottom_t": by_tile(np.asarray(inputs["r_bottom_output"])),
        "w1_pairs": w1_pairs,
        "w1_bottom": np.ascontiguousarray(w1[n_pairs:]),
        "b1": by_partition(inputs["b_top1"]),
        "w2": by_partition(inputs["W_top2"]).reshape(P, H1 // P, H2),
        "b2": np.ascontiguousarray(inputs["b_top2"]),
        "w3": np.ascontiguousarray(inputs["W_top3"]).reshape(-1),
    }
    for f in range(F - 1):
        arrays[f"tbl_{f}"] = np.ascontiguousarray(inputs[f"tbl_{f}"])

    nc = bacc.Bacc("TRN2", target_bir_lowering=False, num_devices=1)
    aps = {name: nc.dram_tensor(name, a.shape, mybir.dt.from_np(a.dtype), kind="ExternalInput").ap()
           for name, a in arrays.items()}
    out = nc.dram_tensor("y", (B, 1), F32, kind="ExternalOutput").ap()
    tables = [aps[f"tbl_{f}"] for f in range(F - 1)]
    program(nc, aps["ids_rows"], aps["ids_cols"], tables, aps["bottom_t"], aps["w1_pairs"], aps["w1_bottom"],
            aps["b1"], aps["w2"], aps["b2"], aps["w3"], out)
    return run_bass_kernel_spmd(nc, [arrays], core_ids=[0]).results[0]["y"]
```
